# Optimizing a Trainium2 kernel written in Bass

```python
import numpy as np
import jax
import jax.numpy as jnp

def _softmax(x, axis=-1):
    return jax.nn.softmax(x, axis=axis)

def _gelu(x):
    return jax.nn.gelu(x, approximate=True)

def _silu(x):
    return jax.nn.silu(x)

def _sigmoid(x):
    return jax.nn.sigmoid(x)

def _layernorm(x, axis=-1, eps=1e-05):
    m = jnp.mean(x, axis=axis, keepdims=True)
    v = jnp.var(x, axis=axis, keepdims=True)
    return (x - m) / jnp.sqrt(v + eps)

def _scatter_add(tgt, idx, src, axis=0):
    return tgt.at[idx].add(src)

def _segment_sum(src, seg, n):
    return jax.ops.segment_sum(src, seg, n)
kernel_name = 'mk_lm_tower_d1_tok_ids2048_r4_aa84c8'

def setup_inputs(seed: int=0):
    np.random.seed(seed)
    _w = jnp.asarray

    def _rec_inputs():
        import jax
        import jax.numpy as jnp
        _rk = jax.random.key(seed)
        x = jax.random.randint(jax.random.fold_in(_rk, 1), (8, 1024), 0, 12564, jnp.int32)
        return x
    x = _rec_inputs()

    def _L0_tok_setup():
        import jax, jax.numpy as jnp
        import numpy as np
        import math
        VOCAB = 50257
        EMBED_DIM = 512
        N_FREQ = 64
        B, T = (8, 512)
        key = jax.random.key(seed)
        ks = jax.random.split(key, 7)
        token_ids = jax.random.randint(ks[0], (B, T), 0, VOCAB)
        init_freqs = jnp.linspace(0.01, 1.0, N_FREQ)[None, :] * jnp.ones((VOCAB, 1))
        frequencies = init_freqs + jax.random.normal(ks[1], (VOCAB, N_FREQ)) * 0.01
        phases = jax.random.normal(ks[2], (VOCAB, N_FREQ)) * 0.1
        amplitudes = jnp.ones((VOCAB, N_FREQ), dtype=jnp.float32)
        lim = 1.0 / math.sqrt(2 * N_FREQ)
        W_proj = jax.random.uniform(ks[3], (EMBED_DIM, 2 * N_FREQ), minval=-lim, maxval=lim)
        b_proj = jax.random.uniform(ks[4], (EMBED_DIM,), minval=-lim, maxval=lim)
        token_bias = jnp.zeros((VOCAB, EMBED_DIM), dtype=jnp.float32)
        return {'token_ids': token_ids, 'frequencies': frequencies, 'phases': phases, 'amplitudes': amplitudes, 'W_proj': W_proj, 'b_proj': b_proj, 'token_bias': token_bias}
    _L0_tok_all = _L0_tok_setup()
    _L0_tok_in = {k: v for k, v in _L0_tok_all.items() if k in ('frequencies', 'phases', 'amplitudes', 'W_proj', 'b_proj', 'token_bias')}
    del _L0_tok_all

    def _L0_attn_setup():
        import jax, jax.numpy as jnp
        import numpy as np
        D_MODEL = 512
        NUM_HEADS = 16
        HEAD_DIM = D_MODEL // NUM_HEADS
        SCALE = HEAD_DIM ** (-0.5)
        ALPHA = 1.0
        key = jax.random.key(seed)
        ks = jax.random.split(key, 9)
        B, T = (2, 512)
        s = 0.02
        w = lambda k: jax.random.normal(k, (D_MODEL, D_MODEL), jnp.float32) * s
        b = lambda k: jax.random.normal(k, (D_MODEL,), jnp.float32) * s
        return {'x': jax.random.normal(ks[0], (B, T, D_MODEL), jnp.float32), 'q_w': w(ks[1]), 'q_b': b(ks[2]), 'k_w': w(ks[3]), 'k_b': b(ks[4]), 'v_w': w(ks[5]), 'v_b': b(ks[6]), 'o_w': w(ks[7]), 'o_b': b(ks[8])}
    _L0_attn_all = _L0_attn_setup()
    _L0_attn_in = {k: v for k, v in _L0_attn_all.items() if k in ('q_w', 'q_b', 'k_w', 'k_b', 'v_w', 'v_b', 'o_w', 'o_b')}
    del _L0_attn_all

    def _L0_ffn_setup():
        import jax, jax.numpy as jnp
        import numpy as np
        E = 32
        K = 6
        H = 512
        I = 256
        T = 512
        CAP = 192
        SCALE = 1.5
        SWIGLU_LIMIT = 10.0
        key = jax.random.key(seed)
        ks = jax.random.split(key, 9)

        def s(k, shape, fan):
            return jax.random.normal(k, shape, jnp.float32) * fan ** (-0.5)
        return {'x': jax.random.normal(ks[0], (1, T, H), jnp.float32), 'gate_w': s(ks[1], (E, H), H), 'bias': jax.random.normal(ks[2], (E,), jnp.float32) * 0.01, 'w_gate': s(ks[3], (E, I, H), H), 'w_up': s(ks[4], (E, I, H), H), 'w_down': s(ks[5], (E, H, I), I), 'sg': s(ks[6], (I, H), H), 'su': s(ks[7], (I, H), H), 'sd': s(ks[8], (H, I), I)}
    _L0_ffn_all = _L0_ffn_setup()
    _L0_ffn_in = {k: v for k, v in _L0_ffn_all.items() if k in ('gate_w', 'bias', 'w_gate', 'w_up', 'w_down', 'sg', 'su', 'sd')}
    del _L0_ffn_all
    return {'x': x, 'L0_tok_frequencies': _L0_tok_in['frequencies'], 'L0_tok_phases': _L0_tok_in['phases'], 'L0_tok_amplitudes': _L0_tok_in['amplitudes'], 'L0_tok_W_proj': _L0_tok_in['W_proj'], 'L0_tok_b_proj': _L0_tok_in['b_proj'], 'L0_tok_token_bias': _L0_tok_in['token_bias'], 'L0_attn_q_w': _L0_attn_in['q_w'], 'L0_attn_q_b': _L0_attn_in['q_b'], 'L0_attn_k_w': _L0_attn_in['k_w'], 'L0_attn_k_b': _L0_attn_in['k_b'], 'L0_attn_v_w': _L0_attn_in['v_w'], 'L0_attn_v_b': _L0_attn_in['v_b'], 'L0_attn_o_w': _L0_attn_in['o_w'], 'L0_attn_o_b': _L0_attn_in['o_b'], 'L0_ffn_gate_w': _L0_ffn_in['gate_w'], 'L0_ffn_bias': _L0_ffn_in['bias'], 'L0_ffn_w_gate': _L0_ffn_in['w_gate'], 'L0_ffn_w_up': _L0_ffn_in['w_up'], 'L0_ffn_w_down': _L0_ffn_in['w_down'], 'L0_ffn_sg': _L0_ffn_in['sg'], 'L0_ffn_su': _L0_ffn_in['su'], 'L0_ffn_sd': _L0_ffn_in['sd']}

def reference(x, L0_tok_frequencies, L0_tok_phases, L0_tok_amplitudes, L0_tok_W_proj, L0_tok_b_proj, L0_tok_token_bias, L0_attn_q_w, L0_attn_q_b, L0_attn_k_w, L0_attn_k_b, L0_attn_v_w, L0_attn_v_b, L0_attn_o_w, L0_attn_o_b, L0_ffn_gate_w, L0_ffn_bias, L0_ffn_w_gate, L0_ffn_w_up, L0_ffn_w_down, L0_ffn_sg, L0_ffn_su, L0_ffn_sd):
    import jax
    import jax.numpy as jnp

    def _L0_tok_ref(token_ids, frequencies, phases, amplitudes, W_proj, b_proj, token_bias):
        import jax, jax.numpy as jnp
        import numpy as np
        import math
        VOCAB = 50257
        EMBED_DIM = 512
        N_FREQ = 64
        B, T = (8, 512)
        freq = frequencies[token_ids]
        phase = phases[token_ids]
        amp = amplitudes[token_ids]
        Tlen = token_ids.shape[1]
        t = jnp.arange(Tlen, dtype=jnp.float32)
        theta = 2.0 * jnp.pi * freq * t[None, :, None] + phase
        sin_c = amp * jnp.sin(theta)
        cos_c = amp * jnp.cos(theta)
        wave_repr = jnp.concatenate([sin_c, cos_c], axis=-1)
        embedded = jnp.einsum('btf,df->btd', wave_repr, W_proj) + b_proj
        return embedded + token_bias[token_ids]

    def _L0_attn_ref(x, q_w, q_b, k_w, k_b, v_w, v_b, o_w, o_b):
        import jax, jax.numpy as jnp
        import numpy as np
        D_MODEL = 512
        NUM_HEADS = 16
        HEAD_DIM = D_MODEL // NUM_HEADS
        SCALE = HEAD_DIM ** (-0.5)
        ALPHA = 1.0
        B, T, D = x.shape
        H, HD = (NUM_HEADS, HEAD_DIM)

        def proj_split(w, bias):
            y = x @ w.T + bias
            return y.reshape(B, T, H, HD).transpose(0, 2, 1, 3).reshape(B * H, T, HD)
        Q = proj_split(q_w, q_b)
        K = proj_split(k_w, k_b)
        V = proj_split(v_w, v_b)
        S = jnp.einsum('hid,hjd->hij', K, Q) * SCALE
        idx = jnp.arange(T)
        delta = idx[:, None] - idx[None, :]
        decay = jnp.where(delta < 0, 0.0, -delta.astype(jnp.float32) ** ALPHA)
        S = jnp.where(delta < 0, -jnp.inf, S) + decay
        C = jax.nn.softmax(S, axis=-1)
        attn = jnp.einsum('hij,hjd->hid', C, V)
        attn = attn.reshape(B, H, T, HD).transpose(0, 2, 1, 3).reshape(B, T, D)
        return attn @ o_w.T + o_b

    def _L0_ffn_ref(x, gate_w, bias, w_gate, w_up, w_down, sg, su, sd):
        import jax, jax.numpy as jnp
        import numpy as np
        E = 32
        K = 6
        H = 512
        I = 256
        T = 512
        CAP = 192
        SCALE = 1.5
        SWIGLU_LIMIT = 10.0
        B, S, Hd = x.shape
        h = x.reshape(-1, Hd)
        logits = h @ gate_w.T
        scores = jnp.sqrt(jax.nn.softplus(logits))
        _, topk_idx = jax.lax.top_k(scores + bias[None, :], K)
        topk_w = jnp.take_along_axis(scores, topk_idx, axis=1)
        topk_w = topk_w / jnp.sum(topk_w, axis=-1, keepdims=True)
        topk_w = topk_w * SCALE
        eid = topk_idx.reshape(-1)
        onehot = jax.nn.one_hot(eid, E, dtype=jnp.int32)
        pos = jnp.cumsum(onehot, axis=0) - 1
        pos = jnp.take_along_axis(pos, eid[:, None], axis=1)[:, 0]
        valid = pos < CAP
        pos = jnp.where(valid, pos, CAP)
        h_rep = jnp.repeat(h, K, axis=0)
        xb = jnp.zeros((E, CAP + 1, Hd), x.dtype).at[eid, pos].set(h_rep)
        g = jnp.einsum('ech,eih->eci', xb, w_gate)
        u = jnp.einsum('ech,eih->eci', xb, w_up)
        inter = jax.nn.silu(g) * u
        yb = jnp.einsum('eci,ehi->ech', inter, w_down)
        w_slot = jnp.where(valid, topk_w.reshape(-1), 0.0)
        y = yb[eid, pos] * w_slot[:, None]
        routed = y.reshape(-1, K, Hd).sum(axis=1)
        si = jax.nn.silu(h @ sg.T) * (h @ su.T)
        si = jnp.clip(si, -SWIGLU_LIMIT, SWIGLU_LIMIT)
        shared = si @ sd.T
        return (routed + shared).reshape(B, S, Hd)
    h = _L0_tok_ref(x, L0_tok_frequencies, L0_tok_phases, L0_tok_amplitudes, L0_tok_W_proj, L0_tok_b_proj, L0_tok_token_bias)
    h = h + _L0_attn_ref(_layernorm(h, axis=-1), L0_attn_q_w, L0_attn_q_b, L0_attn_k_w, L0_attn_k_b, L0_attn_v_w, L0_attn_v_b, L0_attn_o_w, L0_attn_o_b)
    h = h + _L0_ffn_ref(_layernorm(h, axis=-1), L0_ffn_gate_w, L0_ffn_bias, L0_ffn_w_gate, L0_ffn_w_up, L0_ffn_w_down, L0_ffn_sg, L0_ffn_su, L0_ffn_sd)
    return h

_drawn_inputs = setup_inputs


def setup_inputs(seed=0):
    import zlib

    import numpy as np

    out = dict(_drawn_inputs(seed))
    spreads = {'L0_tok_amplitudes': (1.0, 0.2), 'L0_tok_token_bias': (0.0, 0.1)}
    factors = {'L0_attn_q_b': 64.0, 'L0_attn_k_b': 14.194}
    for name, (base, spread) in spreads.items():
        noise = np.random.default_rng([zlib.crc32(name.encode()), seed]).standard_normal(out[name].shape)
        drawn = base * np.exp(spread * noise) if base else spread * noise
        out[name] = jnp.asarray(drawn.astype(out[name].dtype))
    for name, factor in factors.items():
        out[name] = (out[name] * factor).astype(out[name].dtype)
    return out
```

```python
from contextlib import ExitStack

import concourse.bass as bass
from concourse import mybir

F32 = mybir.dt.float32
BF16 = mybir.dt.bfloat16
I32 = mybir.dt.int32
U32 = mybir.dt.uint32
ALU = mybir.AluOpType
ACT = mybir.ActivationFunctionType
AXX = mybir.AxisListType.X
EXP_LN_TABLES = "natural_log_exp_and_others"

P = 128
NB, T = 8, 1024
D = 512
DC = D // P
NF = 64
H, HD = 16, 32
G = H * HD // P
HG = H // G
NT = T // P
E, TOPK, INNER, CAP = 32, 6, 256, 192
MC = INNER // P
HALF = T // 2
SCALE = HD ** -0.5
ROUTED_SCALE = 1.5
LIMIT = 10.0
EPS = 1e-5
NROW = NF * 3 + D
XROW = D + 1 + E
TOKENS = NB * T
SLOT_T = CAP // 2
NEG = -1e30


def wait_from_1(eng, sem, value):
    if isinstance(value, int) and value <= 0:
        return
    eng.wait_ge(sem, value)


def wait_apart(eng, sem, value, passed):
    wait_from_1(eng, sem, value)
    eng.sem_inc(passed, 1)


class Chain:

    def __init__(self, eng, sem, before):
        self.eng, self.sem, self.before, self.n = eng, sem, before, 0

    def done(self, instruction):
        instruction.then_inc(self.sem, 1)
        self.n += 1

    def wait(self):
        wait_from_1(self.eng, self.sem, self.before + self.n)

    def wait_apart(self, passed):
        wait_apart(self.eng, self.sem, self.before + self.n, passed)



TWO_PI = 6.283185307179586
ROUND = 12582912.0
PI_1 = 6.28125
PI_2 = 0.0019353071693331003
PI_3 = TWO_PI - PI_1 - PI_2
PI_BELOW = 3.1415925


def embed(nc, io, dram):
    with ExitStack() as ctx:
        def sb(name, shape, dt=F32):
            return ctx.enter_context(nc.sbuf_tensor("e_" + name, shape, dt))

        def sem(name):
            return ctx.enter_context(nc.semaphore("e_" + name))

        w_proj = sb("w_proj", [P, D])
        ident = sb("ident", [P, P])
        b_proj = sb("b_proj", [P, D])
        b_out = sb("b_out", [P, D])
        one_row = sb("one_row", [1, P])
        position = sb("position", [P, NT])
        half_pi = sb("half_pi", [P, 1])
        eps = sb("eps", [P, 1])
        empty_slots = sb("empty_slots", [SLOT_T, 2, XROW])
        spare = sb("spare", [SLOT_T, 2])
        index_all = sb("index_all", [P, NB * NT], I32)
        index = sb("index", [P, 2, NT], I32)
        rows = [sb(f"rows{p}", [P, NT, NROW]) for p in range(2)]
        theta = sb("theta", [P, NT, NF])
        turns = sb("turns", [P, NT, NF])
        angle = sb("angle", [P, NT, NF])
        angle_abs = sb("angle_abs", [P, NT, NF])
        sines = sb("sines", [P, NT, 2, NF])
        waves = sb("waves", [P, NT, 2 * NF])
        waves_t = sb("waves_t", [P, NT, P])
        hidden = [sb(f"hidden{p}", [P, NT, D]) for p in range(2)]
        stats = sb("stats", [P, NT, 6])
        moments = sb("moments", [P, NT, 2])
        deviation = sb("deviation", [P, NT])
        normed = sb("normed", [P, 4, D])
        normed_t = [sb(f"normed_t{p}", [P, DC, T]) for p in range(2)]
        ps_wave = [ctx.enter_context(nc.psum_tensor(f"e_ps_wave{p}", [P, 512], F32)) for p in range(2)]
        ps_hid = [ctx.enter_context(nc.psum_tensor(f"e_ps_hid{p}", [P, 512], F32)) for p in range(2)]
        ps_tr = [ctx.enter_context(nc.psum_tensor(f"e_ps_tr{p}", [P, 512], F32)) for p in range(2)]

        consts_in = sem("consts_in")
        slots_set = sem("slots_set")
        slots_out = sem("slots_out")
        index_done = sem("index_done")
        rows_in = [sem(f"rows_in{p}") for p in range(2)]
        rows_free = [sem(f"rows_free{p}") for p in range(2)]
        angles_done = sem("angles_done")
        sines_done = sem("sines_done")
        waves_done = sem("waves_done")
        wave_ps_full = sem("wave_ps_full")
        waves_t_done = sem("waves_t_done")
        hid_ps_full = sem("hid_ps_full")
        hidden_done = sem("hidden_done")
        variance_done = sem("variance_done")
        deviation_done = sem("deviation_done")
        normed_done = sem("normed_done")
        tr_ps_full = sem("tr_ps_full")
        normed_t_done = sem("normed_t_done")
        residual_done = sem("residual_done")
        hidden_out = [sem(f"hidden_out{p}") for p in range(2)]
        normed_out = [sem(f"normed_out{p}") for p in range(2)]
        dve_step = sem("dve_step")
        passed = sem("passed")
        DVE_STEPS = 8 + 2 * NT + 1
        N_CONSTS = 7
        TWO = 2

        block = ctx.enter_context(nc.Block())

        @block.sync
        def _(sp):
            for p in range(2):
                sp.sem_inc(hidden_out[p], 16)
                sp.sem_inc(normed_out[p], 16)
            for dst, src in ((w_proj, io["w_projT"]), (ident, io["c_ident"]), (b_proj, io["b_proj"]),
                             (b_out, io["o_b"]), (position, io["c_position"]), (index_all, io["xT"]),
                             (spare, io["c_spare"])):
                sp.dma_start(dst[:], src).then_inc(consts_in, 16)
            sp.wait_ge(slots_set, 2)
            with sp.Fori(0, NB // 2) as pair:
                for k in range(E // (NB // 2)):
                    e = pair * (E // (NB // 2)) + k
                    sp.dma_start(dram["slots"][e].rearrange("(j p) x -> p j x", p=SLOT_T),
                                 empty_slots[:, :, :]).then_inc(slots_out, 16)
                for p in range(2):
                    b = pair * 2 + p
                    sp.wait_ge(residual_done, NT * (b + 1))
                    sp.dma_start(dram["hidden"][b].rearrange("(t p) d -> p t d", p=P),
                                 hidden[p][:]).then_inc(hidden_out[p], 16)
                    sp.wait_ge(normed_t_done, NT * (b + 1) + TWO)
                    sp.dma_start(dram["normed_t"][b], normed_t[p][:]).then_inc(normed_out[p], 16)
            sp.dma_start(io["out"][TOKENS:TOKENS + CAP, :].rearrange("(j p) x -> p j x", p=SLOT_T),
                         empty_slots[:, :, 0:D]).then_inc(slots_out, 16)
            sp.wait_ge(slots_out, 16 * (E + 1))
            for p in range(2):
                sp.wait_ge(hidden_out[p], 16 * (NB // 2) + 16)
                sp.wait_ge(normed_out[p], 16 * (NB // 2) + 16)

        @block.gpsimd
        def _(pool):
            nc.gpsimd.memset(half_pi[:], TWO_PI / 4)
            nc.gpsimd.memset(eps[:], EPS)
            nc.gpsimd.memset(one_row[:], 1.0)
            nc.gpsimd.memset(empty_slots[:], 0.0).then_inc(slots_set, 1)
            pool.wait_ge(consts_in, 16 * N_CONSTS)
            pool.wait_ge(slots_set, 1)
            nc.gpsimd.tensor_copy(empty_slots[:, :, D], spare[:]).then_inc(slots_set, 1)

            def gather(pair, p):
                b = pair * 2 + p
                pool.wait_ge(rows_free[p], pair + 1)
                nc.gpsimd.tensor_copy(index[:, p, :], index_all[:, bass.ds(b * NT, NT)]).then_inc(index_done, 1)
                wait_apart(pool, index_done, b + 1, passed)
                for t in range(NT):
                    nc.gpsimd.indirect_dma_start(
                        rows[p][:, t, :], None, io["table"],
                        bass.IndirectOffsetOnAxis(ap=index[:, p, t:t + 1], axis=0)).then_inc(rows_in[p], 16)

            def add_output_bias(pair, p):
                b = pair * 2 + p
                for t in range(NT):
                    pool.wait_ge(normed_done, NT * b + t + 1)
                    nc.gpsimd.tensor_tensor(hidden[p][:, t, :], hidden[p][:, t, :], b_out[:],
                                            ALU.add).then_inc(residual_done, 1)

            for p in range(2):
                gather(0, p)
            with pool.Fori(0, NB // 2 - 1) as pair:
                for p in range(2):
                    gather(pair + 1, p)
                    add_output_bias(pair, p)
            for p in range(2):
                add_output_bias(NB // 2 - 1, p)

        @block.vector
        def _(dve):
            for p in range(2):
                dve.sem_inc(rows_free[p], 1)
            dve.sem_inc(hidden_done, TWO)
            dve.wait_ge(consts_in, 16 * N_CONSTS)
            with dve.Fori(0, NB // 2) as pair:
                for p in range(2):
                    b = pair * 2 + p
                    chain = Chain(dve, dve_step, DVE_STEPS * b)
                    freq, phase, amp = (rows[p][:, :, k * NF:(k + 1) * NF] for k in range(3))
                    dve.wait_ge(rows_in[p], 16 * NT * (pair + 1))
                    chain.done(nc.vector.scalar_tensor_tensor(
                        theta[:], freq, TWO_PI, position[:].unsqueeze(2).broadcast_to((P, NT, NF)),
                        ALU.mult, ALU.mult))
                    chain.wait()
                    chain.done(nc.vector.tensor_tensor(theta[:], theta[:], phase, ALU.add))
                    chain.wait()
                    chain.done(nc.vector.tensor_scalar(turns[:], theta[:], 1.0 / TWO_PI, ROUND, ALU.mult, ALU.add))
                    chain.wait()
                    chain.done(nc.vector.tensor_scalar(turns[:], turns[:], ROUND, None, ALU.subtract))
                    for part in (PI_1, PI_2, PI_3):
                        chain.wait()
                        chain.done(nc.vector.scalar_tensor_tensor(theta[:], turns[:], -part, theta[:],
                                                                  ALU.mult, ALU.add))
                    chain.wait()
                    chain.done(nc.vector.tensor_scalar(angle[:], theta[:], PI_BELOW, -PI_BELOW, ALU.min, ALU.max))
                    chain.wait()
                    nc.vector.scalar_tensor_tensor(angle_abs[:], angle[:], -1.0, angle[:], ALU.mult, ALU.max).then_inc(angles_done, 1)
                    dve.wait_ge(sines_done, 2 * b + 2)
                    dve.wait_ge(wave_ps_full, 2 * b + TWO)
                    nc.vector.tensor_tensor(waves[:, :, 0:NF], sines[:, :, 0, :], amp, ALU.mult)
                    nc.vector.tensor_tensor(waves[:, :, NF:2 * NF], sines[:, :, 1, :], amp,
                                            ALU.mult).then_inc(waves_done, 1)
                    dve.wait_ge(hidden_out[p], 16 * pair + 16)
                    for t in range(NT):
                        dve.wait_ge(hid_ps_full, NT * b + t + 2)
                        nc.vector.tensor_tensor(hidden[p][:, t, :], ps_hid[t % 2][:], rows[p][:, t, 3 * NF:NROW],
                                                ALU.add).then_inc(hidden_done, 1)
                        dve.wait_ge(hidden_done, NT * b + t + 1 + TWO)
                        chain.done(nc.vector.bn_stats(stats[:, t, :], hidden[p][:, t, :]))
                        chain.wait_apart(passed)
                        chain.done(nc.vector.bn_aggr(moments[:, t, :], stats[:, t, :]))
                    chain.wait()
                    nc.vector.tensor_copy(deviation[:], moments[:, :, 1]).then_inc(variance_done, 1)
                    dve.sem_inc(rows_free[p], 1)
                    dve.wait_ge(deviation_done, b + 1)
                    chain.done(nc.vector.reciprocal(deviation[:], deviation[:]))
                    chain.wait()
                    for t in range(NT):
                        dve.wait_ge(tr_ps_full, NT * b + t + 1)
                        nc.vector.tensor_scalar(normed[:, t % 4, :], hidden[p][:, t, :], moments[:, t, 0:1],
                                                deviation[:, t:t + 1], ALU.subtract, ALU.mult).then_inc(normed_done, 1)
                    assert chain.n == DVE_STEPS, chain.n

        @block.scalar
        def _(act):
            act.sem_inc(waves_t_done, 1)
            act.sem_inc(normed_t_done, TWO)
            with act.Fori(0, NB // 2) as pair:
                for p in range(2):
                    b = pair * 2 + p
                    act.wait_ge(angles_done, b + 1)
                    nc.scalar.activation(sines[:, :, 0, :], angle[:], ACT.Sin).then_inc(sines_done, 1)
                    nc.scalar.activation(sines[:, :, 1, :], angle_abs[:], ACT.Sin, scale=-1.0,
                                         bias=half_pi[:]).then_inc(sines_done, 1)
                    act.wait_ge(hid_ps_full, NT * b + 1)
                    for q in range(2):
                        act.wait_ge(wave_ps_full, 2 * b + q + 1 + TWO)
                        nc.scalar.activation(waves_t[:, 4 * q:4 * q + 4, :],
                                             ps_wave[q][:].rearrange("p (t m) -> p t m", t=4),
                                             ACT.Identity).then_inc(waves_t_done, 1)
                    act.wait_ge(variance_done, b + 1)
                    nc.scalar.activation(deviation[:], deviation[:], ACT.Sqrt, bias=eps[:]).then_inc(deviation_done, 1)
                    act.wait_ge(normed_out[p], 16 * pair + 16)
                    for t in range(NT):
                        act.wait_ge(tr_ps_full, NT * b + t + 5)
                        nc.scalar.activation(normed_t[p][:, :, t * P:(t + 1) * P],
                                             ps_tr[t % 2][:].rearrange("p (c m) -> p c m", c=DC),
                                             ACT.Identity).then_inc(normed_t_done, 1)

        @block.tensor
        def _(pe):
            pe.sem_inc(tr_ps_full, 4)
            pe.sem_inc(wave_ps_full, TWO)
            pe.sem_inc(hid_ps_full, 1)
            pe.wait_ge(consts_in, 16 * N_CONSTS)
            pe.wait_ge(slots_set, 1)
            with pe.Fori(0, NB // 2) as pair:
                for p in range(2):
                    b = pair * 2 + p
                    pe.wait_ge(waves_done, b + 1)
                    pe.wait_ge(waves_t_done, 2 * b + 1)
                    for t in range(NT):
                        mm = nc.tensor.transpose(ps_wave[t // 4][:, (t % 4) * P:(t % 4 + 1) * P], waves[:, t, :], ident[:])
                        if t % 4 == 3:
                            mm.then_inc(wave_ps_full, 1)
                    for t in range(NT):
                        pe.wait_ge(waves_t_done, 2 * b + t // 4 + 2)
                        pe.wait_ge(hidden_done, NT * b + t + 1)
                        nc.tensor.matmul(ps_hid[t % 2][:], waves_t[:, t, :], w_proj[:], start=True, stop=False)
                        nc.tensor.matmul(ps_hid[t % 2][:], one_row[:], b_proj[0:1, :], start=False,
                                         stop=True).then_inc(hid_ps_full, 1)
                    for t in range(NT):
                        pe.wait_ge(normed_done, NT * b + t + 1)
                        pe.wait_ge(normed_t_done, NT * b + t + 1)
                        for c in range(DC):
                            mm = nc.tensor.transpose(ps_tr[t % 2][:, c * P:(c + 1) * P],
                                                     normed[:, t % 4, c * P:(c + 1) * P], ident[:])
                        mm.then_inc(tr_ps_full, 1)


ITEMS = [(half, j, h) for half in range(2) for j in range(NT * (half + 1) // 2) for h in range(HG)]
N_ITEMS = len(ITEMS)
HALF_ITEMS = HG * NT // 2
LAG = 3
FINAL = G * NB
SOFT_LEAST = 2.0 ** -62
N_PROBS = 3
PIECES = HALF // P
ROWS = [(i, h, c) for i in range(NT) for h in range(HG) for c in range(1 + (i >= NT // 2))]
FIRST_LATE_ROW = HG * NT // 2
ROWS_FROM, ROWS_TO = 8, 41
MAX_SLOT = 43
N_ROW_USES = len(ROWS) + 2

PROJECTIONS = [("q", 0), ("k", 0), ("q", 1), ("k", 1), ("v", 0), ("v", 1)]
N_PROJ = len(PROJECTIONS)
QUARTERS = 4
Q_SLOTS = 11


def plan(step_projects, tail):
    slots = [[] for _ in range(N_ITEMS)]
    if tail:
        for q in range(QUARTERS):
            s0 = q * Q_SLOTS
            for j in range(2):
                slots[s0 + j].append(("out", (q, j)))
                slots[s0 + 4 + j].append(("turn", (q, j)))
            slots[s0 + 6].append(("route", (q, 0)))
            for m in range(MC):
                slots[s0 + 7 + m].append(("up", (q, m)))
            for j in range(2):
                slots[s0 + 9].append(("down", (q, j)))
            slots[s0 + 10].append(("place", (q, 0)))
    if step_projects:
        first = 2 if tail else 0
        for k, use in enumerate(PROJECTIONS):
            slots[first + (k // 2 if tail else k)].append(use)
    numbered, n = [], 0
    for slot in slots:
        numbered.append([(kind, arg, n + k) for k, (kind, arg) in enumerate(slot)])
        n += len(slot)
    return numbered


PER_QUARTER = 2 + 2 + 1 + MC + 2 + 1
assert PER_QUARTER * QUARTERS % 2 == 0 and N_PROJ % 2 == 0


def attend(nc, io, dram):
    with ExitStack() as ctx:
        def sb(name, shape, dt=F32):
            return ctx.enter_context(nc.sbuf_tensor("a_" + name, shape, dt))

        def ps(name):
            return ctx.enter_context(nc.psum_tensor("a_" + name, [P, 512], F32))

        def sem(name):
            return ctx.enter_context(nc.semaphore("a_" + name))

        q_w, k_w, v_w, o_w = (sb(n, [P, DC, D]) for n in ("q_w", "k_w", "v_w", "o_w"))
        sg, su = (sb(n, [P, DC, INNER]) for n in ("sg", "su"))
        sd = sb("sd", [P, MC, D])
        router_w = sb("router_w", [P, DC, E])
        v_b = sb("v_b", [P, D])
        q_b, k_b = sb("q_b", [P, G]), sb("k_b", [P, G])
        router_b = sb("router_b", [P, E])
        ident, ident_b = sb("ident", [P, P]), sb("ident_b", [P, P], BF16)
        ones = sb("ones", [P, HD])
        ones_b = sb("ones_b", [P, P], BF16)
        before_b, mask_b = sb("before_b", [P, P], BF16), sb("mask_b", [P, P], BF16)
        experts_row = sb("experts_row", [P, E])
        token = sb("token", [P, 2])
        decay = sb("decay", [P, T])
        S2 = 2 * HD + 5
        q_first, k_first = ([sb(f"{n}_first{p}", [P, HG, T], BF16) for p in range(2)] for n in "qk")
        q_second, k_second = ([sb(f"{n}_second{p}", [P, HG, T], BF16) for p in range(2)] for n in "qk")
        normed_t = sb("normed_t", [P, DC, T])
        values = [sb(f"values{p}", [P, NT, P]) for p in range(2)]
        probs = [sb(f"probs{k}", [P, HALF]) for k in range(N_PROBS)]
        attn_t = sb("attn_t", [P, G, T])
        exact = [sb(f"exact{p}", [P, HALF]) for p in range(2)]
        rest = sb("rest", [P, HALF])
        hi, mid, lo = ([sb(f"{n}{p}", [P, HALF], BF16) for p in range(2)] for n in ("hi", "mid", "lo"))
        row_max = sb("row_max", [P, NT, HG, 2])
        max_cols = sb("max_cols", [P, NT, P], BF16)
        max_rows = sb("max_rows", [P, T], BF16)
        unused = sb("unused", [P, 2, HALF], BF16)
        sum_inv = sb("sum_inv", [P, HALF])
        hidden = [sb(f"hidden{j}", [P, D]) for j in range(2)]
        rows = [sb(f"rows{p}", [P, 2, XROW]) for p in range(2)]
        rows_t = sb("rows_t", [P, DC, 2 * P])
        stats = sb("stats", [P, 2, 6])
        moments = sb("moments", [P, 2, 2])
        rstd, variance, square = sb("rstd", [P, 2]), sb("variance", [P, 2]), sb("square", [P, 2])
        gate_e = sb("gate_e", [P, 2 * P])
        inner_t = sb("inner_t", [P, MC, 2 * P])
        minus_abs, plus, soft_e, soft_w, soft_ln, soft, score, ranked, chosen = (
            sb(n, [P, 2, E]) for n in ("minus_abs", "plus", "soft_e", "soft_w", "soft_ln", "soft", "score",
                                       "ranked", "chosen"))
        top, top_at, top_f = sb("top", [P, 2, 8]), sb("top_at", [P, 2, 8], U32), sb("top_f", [P, 2, 8])
        is_top, at_top = sb("is_top", [P, 2, TOPK, E], BF16), sb("at_top", [P, 2, TOPK, E])
        place, over = sb("place", [P, 2, TOPK]), sb("over", [P, 2, TOPK])
        place_i = [sb(f"place_i{p}", [P, 2, TOPK], I32) for p in range(2)]
        total, total_inv = sb("total", [P, 2]), sb("total_inv", [P, 2])
        chosen_b, counts_b = sb("chosen_b", [P, 2, E], BF16), sb("counts_b", [P, 2, E], BF16)
        counts = sb("counts", [P, E])

        ps_rows = [ps(f"ps_rows{k}") for k in range(2)]
        ps_scores = [ps(f"ps_scores{k}") for k in range(2)]
        ps_attn, ps_sum = ps("ps_attn"), ps("ps_sum")
        ps_dense = [ps(f"ps_dense{k}") for k in range(2)]

        consts_in, consts_made = sem("consts_in"), sem("consts_made")
        normed_in = sem("normed_in")
        dense_full = [sem(f"dense_full{k}") for k in range(2)]
        dense_free = [sem(f"dense_free{k}") for k in range(2)]
        hi_done, rest_done, mid_done, lo_done = (sem(n) for n in ("hi_done", "rest_done", "mid_done", "lo_done"))
        q_parts_out, k_parts_out = sem("q_parts_out"), sem("k_parts_out")
        stacks_in = [sem(f"stacks_in{k}") for k in range(2)]
        rows_full, rows_done, max_done, max_rows_in = (
            sem(n) for n in ("rows_full", "rows_done", "max_done", "max_rows_in"))
        scores_full, exp_done, attn_added = (
            sem(n) for n in ("scores_full", "exp_done", "attn_added"))
        heads_taken, sums_inverted, heads_done = sem("heads_taken"), sem("sums_inverted"), sem("heads_done")
        hidden_in = [sem(f"hidden_in{j}") for j in range(2)]
        out_stored = [sem(f"out_stored{j}") for j in range(2)]
        tail_step = sem("tail_step")
        var_done, rstd_log, rstd_guessed, normed_done = (
            sem(n) for n in ("var_done", "rstd_log", "rstd_guessed", "normed_done"))
        gate_e_done, inner_done = sem("gate_e_done"), sem("inner_done")
        minus_abs_done, soft_e_done, soft_ln_done, soft_done, root_log, root_guessed = (
            sem(n) for n in ("minus_abs_done", "soft_e_done", "soft_ln_done", "soft_done", "root_log", "root_guessed"))
        counted, placed, scattered, rows_free = (sem(n) for n in ("counted", "placed", "scattered", "rows_free"))
        passed = sem("passed")

        consts = [(q_w, "q_w"), (k_w, "k_w"), (v_w, "v_w"), (o_w, "o_w"), (sg, "sg"), (su, "su"), (sd, "sd"),
                  (router_w, "router_w"), (v_b, "v_b"), (q_b, "q_b"), (k_b, "k_b"), (router_b, "router_b"),
                  (ident, "c_ident"), (experts_row, "c_experts"), (token, "c_token"), (decay, "c_decay")]
        before_f = probs[0][:, 0:P]
        query_rows_f = attn_t[2 * HD:S2, 0, :]
        key_rows_f = attn_t[2 * HD:S2, 1, :]
        N_CONSTS = len(consts) + 3
        N_MADE = 3

        FREE = 16
        PART_READS = 16 * 6
        SCATTERS = 16 * 2 * TOPK
        TAIL_STEPS = 47

        def dense_before(s, tails, n):
            return N_PROJ // 2 * (s + 1) + PER_QUARTER * QUARTERS // 2 * tails + n // 2

        def shape(n):
            half, j, h = ITEMS[n]
            i0 = max(half * HALF, j * P)
            return half, j, h, i0, (half + 1) * HALF - i0

        def row_items(n):
            k = N_ROWS_PER(n), N_ROWS_PER(n + 1)
            return range(*k)

        def N_ROWS_PER(n):
            return min(max(n - ROWS_FROM, 0), ROWS_TO - ROWS_FROM) * len(ROWS) // (ROWS_TO - ROWS_FROM)

        def row_shape(k):
            i, h, c = ROWS[k]
            return i, h, c, c * HALF, min((i + 1) * P, (c + 1) * HALF) - c * HALF

        def number_of(uses, kind, arg):
            return next(n for slot in uses for k, a, n in slot if (k, a) == (kind, arg))

        block = ctx.enter_context(nc.Block())

        @block.sync
        def _(sp):
            out_rows = io["out"][0:TOKENS, :].rearrange("(b t) d -> b t d", b=NB)
            for j in range(2):
                sp.sem_inc(out_stored[j], FREE)
            for dst, name in consts:
                sp.dma_start(dst[:], io[name]).then_inc(consts_in, 16)
            sp.dma_start(before_f, io["c_before"]).then_inc(consts_in, 16)
            sp.dma_start(query_rows_f, io["c_query_rows"]).then_inc(consts_in, 16)
            sp.dma_start(key_rows_f, io["c_key_rows"]).then_inc(consts_in, 16)

            def load_normed(b):
                sp.dma_start(normed_t[:], dram["normed_t"][b]).then_inc(normed_in, 16)

            def write_parts(s, p, k):
                cols = slice(k // 2 * HALF, (k // 2 + 1) * HALF)
                parts, order, done = ((dram["q_parts"], (mid, hi, lo), q_parts_out) if k % 2 == 0 else
                                      (dram["k_parts"], (lo, hi, mid, hi), k_parts_out))
                wait_apart(sp, stacks_in[k // 2], PART_READS * (s - 1), passed)
                wait_from_1(sp, lo_done, 4 * s + k + 1)
                for n, src in enumerate(order):
                    sp.dma_start(parts[p, :, n, :, cols], src[k % 2][:]).then_inc(done, 16)

            def read_stacks(s, p, k):
                cols = slice(k // 2 * HALF, (k // 2 + 1) * HALF)
                if k % 2 == 0:
                    src = dram["q_parts"][p].rearrange("h n d t -> (n d) h t")
                    wait_apart(sp, q_parts_out, 16 * 3 * (2 * s + k // 2 + 1), passed)
                    moves = ((q_first, 0, 0), (q_first, 2 * HD, 0), (q_second, 0, HD))
                else:
                    src = dram["k_parts"][p].rearrange("h n d t -> (n d) h t")
                    wait_apart(sp, k_parts_out, 16 * 4 * (2 * s + k // 2 + 1), passed)
                    moves = ((k_first, 0, HD), (k_first, 2 * HD, 2 * HD), (k_second, 0, 0))
                wait_from_1(sp, scores_full, N_ITEMS * (s - 1))
                for dst, to, at in moves:
                    sp.dma_start(dst[p][to:to + 2 * HD, :, cols], src[at:at + 2 * HD, :, cols]).then_inc(stacks_in[k // 2], 16)

            def stacks(s, p):
                write_parts(s, p, 0)
                write_parts(s, p, 1)
                for k in (2, 3):
                    read_stacks(s, p, k - 2)
                    write_parts(s, p, k)
                read_stacks(s, p, 2)
                read_stacks(s, p, 3)

            def move_maxima(s, p):
                wait_from_1(sp, rows_done, N_ROW_USES * (s + 1))
                for h in range(HG):
                    sp.dma_start(k_second[p][2 * HD:2 * HD + 1, h, :],
                                 max_rows[h * HD:h * HD + 1, :]).then_inc(max_rows_in, 16)

            def load_hidden(b, q, j):
                wait_from_1(sp, out_stored[j], FREE + 16 * (QUARTERS * b + q))
                rows_of = slice((2 * q + j) * P, (2 * q + j + 1) * P)
                sp.dma_start(hidden[j][:], dram["hidden"][b, rows_of, :]).then_inc(hidden_in[j], 16)

            def store_out(s, b, q, j, uses):
                n = number_of(uses, "down", (q, j))
                sp.wait_ge(dense_free[n % 2], dense_before(s, b, n) + 1)
                rows_of = slice((2 * q + j) * P, (2 * q + j + 1) * P)
                sp.dma_start(out_rows[b, rows_of, :], hidden[j][:]).then_inc(out_stored[j], 16)

            def tail(s, b, q, uses):
                for j in range(2):
                    store_out(s, b, q, j, uses)
                if q + 1 < QUARTERS:
                    for j in range(2):
                        load_hidden(b, q + 1, j)

            def step(s, g, p, b=None, last=False, tail_b=None):
                uses = plan(not last, tail_b is not None)
                if tail_b is not None:
                    for j in range(2):
                        load_hidden(tail_b, 0, j)
                if not last:
                    stacks(s + 1, 1 - p)
                if g == 2 and b is not None:
                    sp.wait_ge(dense_full[1], dense_before(s, b, 0) + N_PROJ // 2)
                    load_normed(b + 1)
                if tail_b is not None:
                    for q in range(QUARTERS - 1):
                        tail(s, tail_b, q, uses)
                if not last:
                    move_maxima(s + 1, 1 - p)
                if tail_b is not None:
                    tail(s, tail_b, QUARTERS - 1, uses)

            load_normed(0)
            stacks(0, 0)
            move_maxima(0, 0)
            step(0, 0, 0)
            with sp.Fori(0, NB - 1) as b:
                for g in (1, 2, 3):
                    step(b * G + g, g, g % 2, b=b)
                step(b * G + G, 0, 0, tail_b=b)
            for g in (1, 2, 3):
                step((NB - 1) * G + g, g, g % 2, last=(g == G - 1))
            for j in range(2):
                load_hidden(NB - 1, 0, j)
            for q in range(QUARTERS):
                tail(FINAL - 1, NB - 1, q, plan(False, True))
            for j in range(2):
                sp.wait_ge(out_stored[j], FREE + 16 * QUARTERS * NB)
            sp.wait_ge(scattered, SCATTERS * QUARTERS * NB)

        @block.gpsimd
        def _(pool):
            slot_rows = dram["slots"].rearrange("e c x -> (e c) x")
            pool.sem_inc(rows_free, 2)
            nc.gpsimd.memset(ones[:], 1.0)
            nc.gpsimd.memset(ones_b[:], 1.0)
            nc.gpsimd.memset(max_cols[:], 0.0)
            nc.gpsimd.memset(row_max[:], NEG)
            nc.gpsimd.memset(counts[:], 0.0).then_inc(consts_made, 1)

            def split(s, k):
                pool.wait_ge(hi_done, 4 * s + k + 1)
                wait_from_1(pool, mid_done, 4 * s + k)
                wait_from_1(pool, lo_done, 4 * s + k)
                nc.gpsimd.tensor_tensor(rest[:], exact[k % 2][:], hi[k % 2][:], ALU.subtract).then_inc(rest_done, 1)
                pool.wait_ge(mid_done, 4 * s + k + 1)
                nc.gpsimd.tensor_tensor(lo[k % 2][:], rest[:], mid[k % 2][:], ALU.subtract).then_inc(lo_done, 1)

            def scatter(b, q):
                wait_apart(pool, placed, QUARTERS * b + q + 1, passed)
                for j in range(2):
                    for k in range(TOPK):
                        nc.gpsimd.indirect_dma_start(
                            slot_rows, bass.IndirectOffsetOnAxis(ap=place_i[q % 2][:, j, k:k + 1], axis=0), rows[q % 2][:, j, :],
                            None, bounds_check=E * CAP - 1, oob_is_err=False).then_inc(scattered, 16)

            def scatter_through(b, q):
                pool.wait_ge(scattered, SCATTERS * (QUARTERS * b + q + 1))
                pool.sem_inc(rows_free, 1)

            def step(s, last=False, tail_b=None):
                uses = plan(not last, tail_b is not None)
                for n in range(N_ITEMS):
                    for kind, arg, _ in uses[n]:
                        if kind in ("q", "k"):
                            split(s + 1, 2 * arg + (kind == "k"))
                    if tail_b is not None and n > 0 and n % Q_SLOTS == 0:
                        q = n // Q_SLOTS - 1
                        if q > 0:
                            scatter_through(tail_b, q - 1)
                        scatter(tail_b, q)
                if tail_b is not None:
                    scatter_through(tail_b, QUARTERS - 1)

            for k in range(4):
                split(0, k)
            step(0)
            with pool.Fori(0, NB - 1) as b:
                for g in (1, 2, 3):
                    step(b * G + g)
                step(b * G + G, tail_b=b)
            for g in (1, 2, 3):
                step((NB - 1) * G + g, last=(g == G - 1))
            for q in range(QUARTERS):
                scatter(NB - 1, q)
                scatter_through(NB - 1, q)

        @block.scalar
        def _(act):
            act.preload_act_table_set(EXP_LN_TABLES)
            act.wait_ge(consts_in, 16 * N_CONSTS)
            nc.scalar.mul(q_b[:], q_b[:], SCALE).then_inc(consts_made, 1)
            act.wait_ge(consts_made, N_MADE)

            def take_projection(s, g, k, bank, before):
                wait_from_1(act, rest_done, 4 * s + k - 1)
                act.wait_ge(dense_full[bank], before + 1)
                bias, scale = (q_b, SCALE) if k % 2 == 0 else (k_b, 1.0)
                nc.scalar.activation(exact[k % 2][:], ps_dense[bank][:], ACT.Identity, bias=bias[:, g:g + 1],
                                     scale=scale).then_inc(dense_free[bank], 1)

            def soften(s, n):
                width = shape(n)[4]
                wait_from_1(act, attn_added, N_ITEMS * s + n - N_PROBS + 1)
                act.wait_ge(scores_full, N_ITEMS * s + n + 1)
                nc.scalar.activation(probs[n % N_PROBS][:, 0:width], ps_scores[n % 2][:, 0:width],
                                     ACT.Exp).then_inc(exp_done, 1)

            def take_heads(s, g, half, items, waits=()):
                wait_from_1(act, heads_done, 2 * s + half)
                for semaphore, value in waits:
                    act.wait_ge(semaphore, value)
                act.wait_ge(attn_added, items)
                nc.scalar.activation(sum_inv[:], ps_sum[:], ACT.Identity)
                nc.scalar.activation(attn_t[:, g, half * HALF:(half + 1) * HALF], ps_attn[:],
                                     ACT.Identity).then_inc(heads_taken, 1)

            def guess_rstd(x):
                act.wait_ge(var_done, x + 1)
                nc.scalar.activation(rstd[:], variance[:], ACT.Ln).then_inc(rstd_log, 1)
                act.wait_ge(rstd_log, x + 1)
                nc.scalar.activation(rstd[:], rstd[:], ACT.Exp, scale=-0.5).then_inc(rstd_guessed, 1)

            def take_turned(j, bank, before):
                act.wait_ge(dense_full[bank], before + 1)
                nc.scalar.activation(rows_t[:, :, j * P:(j + 1) * P],
                                     ps_dense[bank][:].rearrange("p (c m) -> p c m", c=DC),
                                     ACT.Identity).then_inc(dense_free[bank], 1)

            def soften_gate(x, m, bank, before):
                wait_from_1(act, inner_done, MC * x + m)
                act.wait_ge(dense_full[bank], before + 1)
                nc.scalar.activation(gate_e[:], ps_dense[bank][:, 0:2 * P], ACT.Exp, scale=-1.0).then_inc(gate_e_done, 1)

            def soft_plus(x):
                act.wait_ge(minus_abs_done, x + 1)
                nc.scalar.activation(soft_e[:], minus_abs[:], ACT.Exp).then_inc(soft_e_done, 1)
                act.wait_ge(soft_e_done, x + 1)
                nc.scalar.activation(soft_ln[:], soft_e[:], ACT.Ln, bias=1.0).then_inc(soft_ln_done, 1)

            def guess_root(x):
                act.wait_ge(soft_done, x + 1)
                nc.scalar.activation(score[:], soft[:], ACT.Ln).then_inc(root_log, 1)
                act.wait_ge(root_log, x + 1)
                nc.scalar.activation(score[:], score[:], ACT.Exp, scale=0.5).then_inc(root_guessed, 1)

            def dense(s, g, tails, slot, tail_b):
                for kind, arg, n in slot:
                    bank, before = n % 2, dense_before(s, tails, n)
                    if kind in ("q", "k"):
                        take_projection(s + 1, g, 2 * arg + (kind == "k"), bank, before)
                        continue
                    if kind == "v":
                        continue
                    q, j = arg
                    x = tail_b * QUARTERS + q
                    if kind == "out" and j == 1:
                        guess_rstd(x)
                    elif kind == "turn":
                        take_turned(j, bank, before)
                    elif kind == "route":
                        soft_plus(x)
                    elif kind == "up":
                        soften_gate(x, j, bank, before)
                        if j == 0:
                            guess_root(x)

            def step(s, g, tails, first=False, last=False, tail_b=None):
                uses = plan(not last, tail_b is not None)
                for n in range(N_ITEMS):
                    soften(s, n)
                    if n == LAG - 1 and not first:
                        waits = [(dense_full[k], dense_before(s, tails, 0)) for k in range(2)] if g == 1 else ()
                        take_heads(s - 1, (g - 1) % G, 1, N_ITEMS * s, waits)
                    if n == HALF_ITEMS + LAG - 1:
                        waits = ()
                        if tail_b is not None:
                            n_out = number_of(uses, "out", (1, 1))
                            waits = [(dense_full[n_out % 2], dense_before(s, tails, n_out) + 1)]
                        take_heads(s, g, 0, N_ITEMS * s + HALF_ITEMS, waits)
                    dense(s, (g + 1) % G, tails, uses[n], tail_b)

            for k, (kind, half) in enumerate(PROJECTIONS[:4]):
                take_projection(0, 0, 2 * half + (kind == "k"), k % 2, k // 2)
            step(0, 0, 0, first=True)
            with act.Fori(0, NB - 1) as b:
                for g in (1, 2, 3):
                    step(b * G + g, g, b)
                step(b * G + G, 0, b, tail_b=b)
            for g in (1, 2, 3):
                step((NB - 1) * G + g, g, NB - 1, last=(g == G - 1))
            take_heads(FINAL - 1, G - 1, 1, N_ITEMS * FINAL)
            for slot in plan(False, True):
                dense(FINAL - 1, 0, NB - 1, slot, NB - 1)

        @block.vector
        def _(dve):
            dve.wait_ge(consts_in, 16 * N_CONSTS)
            nc.vector.tensor_copy(ident_b[:], ident[:])
            nc.vector.tensor_copy(before_b[:], before_f)
            nc.vector.tensor_scalar(mask_b[:], before_f, NEG, None, ALU.mult)
            for p in range(2):
                for h in range(HG):
                    nc.vector.tensor_copy(q_second[p][2 * HD:S2, h, :], query_rows_f)
                    last_copy = nc.vector.tensor_copy(k_second[p][2 * HD:S2, h, :], key_rows_f)
            last_copy.then_inc(consts_made, 1)
            dve.wait_ge(consts_made, N_MADE)

            def split(s, k, bank, before):
                done = q_parts_out if k % 2 == 0 else k_parts_out
                dve.wait_ge(dense_free[bank], before + 1)
                wait_from_1(dve, done, (3 if k % 2 == 0 else 4) * 16 * (2 * s + k // 2))
                nc.vector.tensor_copy(hi[k % 2][:], exact[k % 2][:]).then_inc(hi_done, 1)
                dve.wait_ge(rest_done, 4 * s + k + 1)
                nc.vector.tensor_copy(mid[k % 2][:], rest[:]).then_inc(mid_done, 1)

            def take_values(s, g, p, half, bank, before):
                wait_from_1(dve, attn_added, N_ITEMS * (s - 1))
                dve.wait_ge(dense_full[bank], before + 1)
                nc.vector.tensor_tensor(values[p][:, 4 * half:4 * half + 4, :],
                                        ps_dense[bank][:].rearrange("p (t m) -> p t m", t=4),
                                        v_b[:, g * P:(g + 1) * P].unsqueeze(1).broadcast_to((P, 4, P)),
                                        ALU.add).then_inc(dense_free[bank], 1)

            def row_maximum(s, k):
                i, h, c, j0, width = row_shape(k)
                if k == 0:
                    wait_apart(dve, max_done, s, passed)
                wait_apart(dve, rows_full, N_ROW_USES * s + k + 1, passed)
                at = T - P - i * P + j0
                nc.vector.tensor_tensor_reduce(unused[:, k % 2, 0:width], ps_rows[k % 2][:, 0:width],
                                               decay[:, at:at + width], 1.0, NEG, ALU.add, ALU.max,
                                               row_max[:, i, h, c:c + 1]).then_inc(rows_done, 1)

            def maxima(s):
                dve.wait_ge(rows_done, N_ROW_USES * s + len(ROWS))
                cols = max_cols[:].rearrange("p i (h d) -> p i h d", d=HD)[:, :, :, 0]
                nc.vector.tensor_tensor(cols, row_max[:, :, :, 0], row_max[:, :, :, 1], ALU.max).then_inc(max_done, 1)
                wait_from_1(dve, max_rows_in, 16 * HG * s)
                for k in range(2):
                    dve.wait_ge(rows_full, N_ROW_USES * s + len(ROWS) + k + 1)
                    nc.vector.tensor_copy(max_rows[:, k * HALF:(k + 1) * HALF], ps_rows[k][:]).then_inc(rows_done, 1)

            def divide_heads(s, g, half, piece):
                cols = slice(piece * P, (piece + 1) * P)
                heads = attn_t[:, g, half * HALF + piece * P:half * HALF + (piece + 1) * P]
                dve.wait_ge(heads_taken, 2 * s + half + 1)
                nc.vector.reciprocal(sum_inv[:, cols], sum_inv[:, cols]).then_inc(sums_inverted, 1)
                dve.wait_ge(sums_inverted, PIECES * (2 * s + half) + piece + 1)
                instruction = nc.vector.tensor_tensor(heads, heads, sum_inv[:, cols], ALU.mult)
                if piece == PIECES - 1:
                    instruction.then_inc(heads_done, 1)

            def add_residual(x, j, bank, before, chain):
                dve.wait_ge(hidden_in[j], 16 * (x + 1))
                dve.wait_ge(dense_full[bank], before + 1)
                nc.vector.tensor_tensor(hidden[j][:], ps_dense[bank][:], hidden[j][:], ALU.add).then_inc(dense_free[bank], 1)
                dve.wait_ge(dense_free[bank], before + 1)
                chain.done(nc.vector.bn_stats(stats[:, j, :], hidden[j][:]))
                chain.wait_apart(passed)
                chain.done(nc.vector.bn_aggr(moments[:, j, :], stats[:, j, :]))
                if j == 1:
                    chain.wait()
                    nc.vector.tensor_scalar(variance[:], moments[:, :, 1], EPS, None, ALU.add).then_inc(var_done, 1)

            def normalise(x, x_rows, chain):
                dve.wait_ge(rstd_guessed, x + 1)
                chain.done(nc.vector.tensor_tensor(square[:], rstd[:], rstd[:], ALU.mult))
                chain.wait()
                chain.done(nc.vector.tensor_tensor(square[:], square[:], variance[:], ALU.mult))
                chain.wait()
                chain.done(nc.vector.tensor_scalar(square[:], square[:], -0.5, 1.5, ALU.mult, ALU.add))
                chain.wait()
                chain.done(nc.vector.tensor_tensor(rstd[:], rstd[:], square[:], ALU.mult))
                chain.wait()
                dve.wait_ge(rows_free, x + 1)
                for j in range(2):
                    nc.vector.tensor_scalar(rows[x_rows][:, j, 0:D], hidden[j][:], moments[:, j, 0:1], rstd[:, j:j + 1],
                                            ALU.subtract, ALU.mult).then_inc(normed_done, 1)

            def soft_parts(x, bank, before, chain):
                logits = ps_dense[bank][:, 0:2 * E].rearrange("p (j e) -> p j e", j=2)
                dve.wait_ge(dense_full[bank], before + 1)
                chain.done(nc.vector.tensor_scalar(plus[:], logits, 0.0, None, ALU.max))
                nc.vector.tensor_scalar(minus_abs[:], logits, 0.0, None, ALU.min).then_inc(dense_free[bank], 1)
                chain.wait()
                dve.wait_ge(dense_free[bank], before + 1)
                nc.vector.tensor_tensor(minus_abs[:], minus_abs[:], plus[:], ALU.subtract).then_inc(minus_abs_done, 1)

            def soft_sum(x, chain):
                dve.wait_ge(soft_e_done, x + 1)
                chain.done(nc.vector.tensor_scalar(soft_w[:], soft_e[:], 1.0, None, ALU.add))
                chain.wait()
                chain.done(nc.vector.scalar_tensor_tensor(soft[:], soft_w[:], 1.0, soft_e[:], ALU.subtract, ALU.subtract))
                chain.done(nc.vector.reciprocal(soft_w[:], soft_w[:]))
                chain.wait()
                chain.done(nc.vector.tensor_tensor(soft[:], soft[:], soft_w[:], ALU.mult))
                dve.wait_ge(soft_ln_done, x + 1)
                chain.wait()
                chain.done(nc.vector.tensor_tensor(soft[:], soft_ln[:], soft[:], ALU.subtract))
                chain.wait()
                chain.done(nc.vector.tensor_tensor(soft[:], soft[:], plus[:], ALU.add))
                chain.wait()
                nc.vector.tensor_scalar(soft[:], soft[:], SOFT_LEAST, None, ALU.max).then_inc(soft_done, 1)

            def choose(x, chain):
                dve.wait_ge(root_guessed, x + 1)
                chain.done(nc.vector.reciprocal(soft_w[:], score[:]))
                chain.wait()
                chain.done(nc.vector.tensor_tensor(soft_w[:], soft_w[:], soft[:], ALU.mult))
                chain.wait()
                chain.done(nc.vector.tensor_tensor(soft_w[:], soft_w[:], score[:], ALU.add))
                chain.wait()
                chain.done(nc.vector.tensor_scalar(score[:], soft_w[:], 0.5, None, ALU.mult))
                chain.wait()
                chain.done(nc.vector.tensor_tensor(ranked[:], score[:], router_b[:].unsqueeze(1).broadcast_to((P, 2, E)),
                                                   ALU.add))
                chain.wait_apart(passed)
                for j in range(2):
                    chain.done(nc.vector.max(top[:, j, :], ranked[:, j, :]))
                chain.wait_apart(passed)
                for j in range(2):
                    chain.done(nc.vector.max_index(top_at[:, j, :], top[:, j, :], ranked[:, j, :]))
                chain.wait()
                chain.done(nc.vector.tensor_copy(top_f[:], top_at[:]))
                chain.wait()
                chain.done(nc.vector.tensor_tensor(
                    is_top[:], experts_row[:].unsqueeze(1).unsqueeze(1).broadcast_to((P, 2, TOPK, E)),
                    top_f[:, :, 0:TOPK].unsqueeze(3).broadcast_to((P, 2, TOPK, E)), ALU.is_equal))
                chain.wait()
                chain.done(nc.vector.tensor_reduce(chosen[:], is_top[:].rearrange("p j k e -> p j e k"), AXX, ALU.add))
                chain.wait()
                chain.done(nc.vector.tensor_copy(chosen_b[:], chosen[:]))
                for j in range(2):
                    chain.done(nc.vector.tensor_copy(counts_b[:, j, :], counts[:]))
                    chain.wait()
                    instruction = nc.vector.tensor_tensor(counts[:], counts[:], chosen[:, j, :], ALU.add)
                    if j == 0:
                        chain.done(instruction)
                        chain.wait()
                    else:
                        instruction.then_inc(counted, 1)

            def find_places(x, x_rows, bank, before, chain):
                earlier = ps_dense[bank][:, 0:2 * E].rearrange("p (j e) -> p j e", j=2)
                dve.wait_ge(dense_full[bank], before + 1)
                nc.vector.tensor_tensor(at_top[:], is_top[:], earlier.unsqueeze(2).broadcast_to((P, 2, TOPK, E)),
                                        ALU.mult).then_inc(dense_free[bank], 1)
                chain.done(nc.vector.tensor_tensor(chosen[:], chosen[:], score[:], ALU.mult))
                chain.wait()
                chain.done(nc.vector.tensor_reduce(total[:], chosen[:], AXX, ALU.add))
                dve.wait_ge(dense_free[bank], before + 1)
                chain.done(nc.vector.tensor_reduce(place[:], at_top[:], AXX, ALU.add))
                chain.wait()
                chain.done(nc.vector.reciprocal(total_inv[:], total[:]))
                chain.done(nc.vector.tensor_scalar(over[:], place[:], float(CAP), float(E * CAP), ALU.is_ge, ALU.mult))
                chain.done(nc.vector.scalar_tensor_tensor(place[:], top_f[:, :, 0:TOPK], float(CAP), place[:],
                                                          ALU.mult, ALU.add))
                chain.wait()
                for j in range(2):
                    chain.done(nc.vector.tensor_scalar(rows[x_rows][:, j, D + 1:XROW], chosen[:, j, :], total_inv[:, j:j + 1],
                                                       ROUTED_SCALE, ALU.mult, ALU.mult))
                chain.done(nc.vector.tensor_copy(rows[x_rows][:, :, D], token[:]))
                chain.done(nc.vector.tensor_tensor(place[:], place[:], over[:], ALU.add))
                chain.wait()
                nc.vector.tensor_scalar(token[:], token[:], float(2 * P), None, ALU.add)
                nc.vector.tensor_copy(place_i[x_rows][:], place[:]).then_inc(placed, 1)

            def gate(x, m, bank, before, chain):
                g, u = ps_dense[bank][:, 0:2 * P], ps_dense[bank][:, 2 * P:4 * P]
                dve.wait_ge(gate_e_done, MC * x + m + 1)
                chain.done(nc.vector.tensor_scalar(gate_e[:], gate_e[:], 1.0, None, ALU.add))
                chain.wait()
                chain.done(nc.vector.reciprocal(gate_e[:], gate_e[:]))
                chain.wait()
                chain.done(nc.vector.tensor_tensor(gate_e[:], g, gate_e[:], ALU.mult))
                chain.wait()
                nc.vector.tensor_tensor(gate_e[:], u, gate_e[:], ALU.mult).then_inc(dense_free[bank], 1)
                dve.wait_ge(dense_free[bank], before + 1)
                nc.vector.tensor_scalar(inner_t[:, m, :], gate_e[:], LIMIT, -LIMIT, ALU.min, ALU.max).then_inc(inner_done, 1)

            def add_shared(j, bank, before):
                dve.wait_ge(dense_full[bank], before + 1)
                nc.vector.tensor_tensor(hidden[j][:], ps_dense[bank][:], hidden[j][:], ALU.add).then_inc(dense_free[bank], 1)

            def dense(s, g, p, tails, slot, tail_b, chains):
                for kind, arg, n in slot:
                    bank, before = n % 2, dense_before(s, tails, n)
                    if kind in ("q", "k"):
                        split(s + 1, 2 * arg + (kind == "k"), bank, before)
                        continue
                    if kind == "v":
                        take_values(s + 1, g, p, arg, bank, before)
                        continue
                    q, j = arg
                    x = tail_b * QUARTERS + q
                    if kind == "out" and j == 0:
                        chains[q] = Chain(dve, tail_step, x * TAIL_STEPS)
                    chain = chains[q]
                    if kind == "out":
                        add_residual(x, j, bank, before, chain)
                    elif kind == "route":
                        soft_parts(x, bank, before, chain)
                    elif kind == "up":
                        if j == 0:
                            soft_sum(x, chain)
                        gate(x, j, bank, before, chain)
                        if j == 1:
                            choose(x, chain)
                    elif kind == "down":
                        add_shared(j, bank, before)
                    elif kind == "place":
                        find_places(x, q % 2, bank, before, chain)
                        assert chain.n == TAIL_STEPS, chain.n

            def tail_slot(n, tail_b, chains):
                if tail_b is not None and n % Q_SLOTS == 2 and n // Q_SLOTS < QUARTERS:
                    q = n // Q_SLOTS
                    normalise(tail_b * QUARTERS + q, q % 2, chains[q])

            def step(s, g, p, tails, first=False, last=False, tail_b=None):
                uses = plan(not last, tail_b is not None)
                chains = {}
                for n in range(N_ITEMS):
                    if not last:
                        for k in row_items(n):
                            row_maximum(s + 1, k)
                    if LAG <= n < LAG + PIECES and not first:
                        divide_heads(s - 1, (g - 1) % G, 1, n - LAG)
                    if HALF_ITEMS + LAG <= n < HALF_ITEMS + LAG + PIECES:
                        divide_heads(s, g, 0, n - HALF_ITEMS - LAG)
                    tail_slot(n, tail_b, chains)
                    dense(s, (g + 1) % G, 1 - p, tails, uses[n], tail_b, chains)
                    if n == MAX_SLOT and not last:
                        maxima(s + 1)

            for k, (kind, half) in enumerate(PROJECTIONS):
                if kind == "v":
                    take_values(0, 0, 0, half, k % 2, k // 2)
                else:
                    split(0, 2 * half + (kind == "k"), k % 2, k // 2)
            for k in range(len(ROWS)):
                row_maximum(0, k)
            maxima(0)
            step(0, 0, 0, 0, first=True)
            with dve.Fori(0, NB - 1) as b:
                for g in (1, 2, 3):
                    step(b * G + g, g, g % 2, b)
                step(b * G + G, 0, 0, b, tail_b=b)
            for g in (1, 2, 3):
                step((NB - 1) * G + g, g, g % 2, NB - 1, last=(g == G - 1))
            for piece in range(PIECES):
                divide_heads(FINAL - 1, G - 1, 1, piece)
            chains = {}
            for n, slot in enumerate(plan(False, True)):
                tail_slot(n, NB - 1, chains)
                dense(FINAL - 1, 0, 0, NB - 1, slot, NB - 1, chains)

        @block.tensor
        def _(pe):
            pe.wait_ge(consts_in, 16 * N_CONSTS)
            pe.wait_ge(consts_made, N_MADE)

            def project(s, g, kind, half, bank, before):
                wait_from_1(pe, dense_free[bank], before)
                w = {"q": q_w, "k": k_w, "v": v_w}[kind]
                if kind == "v":
                    for t in range(NT // 2):
                        tile = half * NT // 2 + t
                        for c in range(DC):
                            mm = nc.tensor.matmul(ps_dense[bank][:, t * P:(t + 1) * P], normed_t[:, c, tile * P:(tile + 1) * P],
                                                  w[:, c, g * P:(g + 1) * P], start=(c == 0), stop=(c == DC - 1))
                else:
                    for c in range(DC):
                        mm = nc.tensor.matmul(ps_dense[bank][:], w[:, c, g * P:(g + 1) * P],
                                              normed_t[:, c, half * HALF:(half + 1) * HALF],
                                              start=(c == 0), stop=(c == DC - 1))
                mm.then_inc(dense_full[bank], 1)

            def row_scores(s, p, k):
                i, h, c, j0, width = row_shape(k)
                if k == 0:
                    pe.wait_ge(stacks_in[0], PART_READS * (s + 1))
                if k == FIRST_LATE_ROW:
                    pe.wait_ge(stacks_in[1], PART_READS * (s + 1))
                wait_from_1(pe, rows_done, N_ROW_USES * s + k - 1)
                nc.tensor.matmul(ps_rows[k % 2][:, 0:width], k_first[p][:, h, i * P:(i + 1) * P],
                                 q_first[p][:, h, j0:j0 + width], start=True, stop=True).then_inc(rows_full, 1)

            def turn_maxima(s):
                pe.wait_ge(max_done, s + 1)
                for k in range(2):
                    pe.wait_ge(rows_done, N_ROW_USES * s + len(ROWS) + k - 1)
                    for i in range(NT // 2):
                        mm = nc.tensor.matmul(ps_rows[k][:, i * P:(i + 1) * P], max_cols[:, k * NT // 2 + i, :],
                                              ident_b[:], start=True, stop=True)
                    mm.then_inc(rows_full, 1)

            def scores(s, p, n):
                half, j, h, i0, width = shape(n)
                if n == 0:
                    pe.wait_ge(max_rows_in, 16 * HG * (s + 1))
                wait_from_1(pe, exp_done, N_ITEMS * s + n - 1)
                nc.tensor.matmul(ps_scores[n % 2][:, 0:width], q_first[p][:, h, j * P:(j + 1) * P],
                                 k_first[p][:, h, i0:i0 + width], start=True, stop=False)
                if j * P == i0:
                    nc.tensor.matmul(ps_scores[n % 2][:, 0:P], mask_b[:], ident_b[:], start=False, stop=False)
                nc.tensor.matmul(ps_scores[n % 2][:, 0:width], q_second[p][0:S2, h, j * P:(j + 1) * P],
                                 k_second[p][0:S2, h, i0:i0 + width], start=False, stop=True).then_inc(scores_full, 1)

            def attend_item(s, p, n, tails):
                half, j, h, i0, width = shape(n)
                if n == 0:
                    for k in range(2):
                        wait_from_1(pe, dense_free[k], dense_before(s, tails, 0))
                if n % HALF_ITEMS == 0 and n <= HALF_ITEMS:
                    wait_from_1(pe, heads_taken, 2 * s + half)
                pe.wait_ge(exp_done, N_ITEMS * s + n + 1)
                at = slice(i0 - half * HALF, i0 - half * HALF + width)
                heads = slice(h * HD, (h + 1) * HD)
                last_j = (half + 1) * NT // 2 - 1
                nc.tensor.matmul(ps_attn[heads, at], values[p][:, j, heads], probs[n % N_PROBS][:, 0:width],
                                 start=(j == 0), stop=(j == last_j))
                nc.tensor.matmul(ps_sum[heads, at], ones[:], probs[n % N_PROBS][:, 0:width],
                                 start=(j == 0), stop=(j == last_j)).then_inc(attn_added, 1)

            def out_project(b, q, j, bank, before):
                wait_from_1(pe, dense_free[bank], before)
                pe.wait_ge(heads_done, 2 * G * b + 2 * G - (1 if q < QUARTERS // 2 else 0))
                tile = 2 * q + j
                for g in range(G):
                    mm = nc.tensor.matmul(ps_dense[bank][:], attn_t[:, g, tile * P:(tile + 1) * P], o_w[:, g, :],
                                          start=(g == 0), stop=(g == G - 1))
                mm.then_inc(dense_full[bank], 1)

            def turn(x, x_rows, j, bank, before):
                wait_from_1(pe, dense_free[bank], before)
                pe.wait_ge(normed_done, 2 * x + j + 1)
                for c in range(DC):
                    mm = nc.tensor.transpose(ps_dense[bank][:, c * P:(c + 1) * P], rows[x_rows][:, j, c * P:(c + 1) * P], ident[:])
                mm.then_inc(dense_full[bank], 1)

            def route(bank, before):
                wait_from_1(pe, dense_free[bank], before)
                for j in range(2):
                    for c in range(DC):
                        mm = nc.tensor.matmul(ps_dense[bank][:, j * E:(j + 1) * E], rows_t[:, c, j * P:(j + 1) * P],
                                              router_w[:, c, :], start=(c == 0), stop=(c == DC - 1))
                mm.then_inc(dense_full[bank], 1)

            def up(m, bank, before):
                wait_from_1(pe, dense_free[bank], before)
                for k, w in enumerate((sg, su)):
                    for c in range(DC):
                        mm = nc.tensor.matmul(ps_dense[bank][:, k * 2 * P:(k + 1) * 2 * P], w[:, c, m * P:(m + 1) * P],
                                              rows_t[:, c, :], start=(c == 0), stop=(c == DC - 1))
                mm.then_inc(dense_full[bank], 1)

            def down(x, j, bank, before):
                wait_from_1(pe, dense_free[bank], before)
                pe.wait_ge(inner_done, MC * (x + 1))
                for m in range(MC):
                    mm = nc.tensor.matmul(ps_dense[bank][:], inner_t[:, m, j * P:(j + 1) * P], sd[:, m, :],
                                          start=(m == 0), stop=(m == MC - 1))
                mm.then_inc(dense_full[bank], 1)

            def count_earlier(x, bank, before):
                wait_from_1(pe, dense_free[bank], before)
                pe.wait_ge(counted, x + 1)
                nc.tensor.matmul(ps_dense[bank][:, 0:2 * E], before_b[:], chosen_b[:].rearrange("p j e -> p (j e)"),
                                 start=True, stop=False)
                nc.tensor.matmul(ps_dense[bank][:, 0:2 * E], ones_b[:], counts_b[:].rearrange("p j e -> p (j e)"),
                                 start=False, stop=True).then_inc(dense_full[bank], 1)

            def dense(s, g, tails, uses, slot, tail_b):
                for kind, arg, n in slot:
                    bank, before = n % 2, dense_before(s, tails, n)
                    if kind in ("q", "k", "v"):
                        project(s + 1, g, kind, arg, bank, before)
                        continue
                    q, j = arg
                    x = tail_b * QUARTERS + q
                    if kind == "out":
                        out_project(tail_b, q, j, bank, before)
                    elif kind == "turn":
                        turn(x, q % 2, j, bank, before)
                    elif kind == "route":
                        for k in range(2):
                            n_turn = number_of(uses, "turn", (q, k))
                            pe.wait_ge(dense_free[n_turn % 2], dense_before(s, tails, n_turn) + 1)
                        route(bank, before)
                    elif kind == "up":
                        up(j, bank, before)
                    elif kind == "down":
                        down(x, j, bank, before)
                    elif kind == "place":
                        count_earlier(x, bank, before)

            def step(s, g, p, tails, first=False, last=False, tail_b=None, b_next=None):
                uses = plan(not last, tail_b is not None)
                for n in range(N_ITEMS):
                    items = row_items(n) if not last else ()
                    if b_next is not None and n == 0:
                        pe.wait_ge(normed_in, 16 * (b_next + 1))
                    if n == 0:
                        dense(s, (g + 1) % G, tails, uses, uses[n], tail_b)
                    scores(s, p, n)
                    for k in items[:1]:
                        row_scores(s + 1, 1 - p, k)
                    if n >= LAG:
                        attend_item(s, p, n - LAG, tails)
                    elif not first:
                        attend_item(s - 1, 1 - p, N_ITEMS + n - LAG, tails)
                    for k in items[1:]:
                        row_scores(s + 1, 1 - p, k)
                    if n > 0:
                        dense(s, (g + 1) % G, tails, uses, uses[n], tail_b)
                    if n == MAX_SLOT and not last:
                        turn_maxima(s + 1)

            pe.wait_ge(normed_in, 16)
            for k, (kind, half) in enumerate(PROJECTIONS):
                project(0, 0, kind, half, k % 2, k // 2)
            for k in range(len(ROWS)):
                row_scores(0, 0, k)
            turn_maxima(0)
            step(0, 0, 0, 0, first=True)
            with pe.Fori(0, NB - 1) as b:
                for g in (1, 2, 3):
                    step(b * G + g, g, g % 2, b, b_next=(b + 1 if g == 3 else None))
                step(b * G + G, 0, 0, b, tail_b=b)
            for g in (1, 2, 3):
                step((NB - 1) * G + g, g, g % 2, NB - 1, last=(g == G - 1))
            for k in range(LAG):
                attend_item(FINAL - 1, 1, N_ITEMS + k - LAG, NB - 1)
            uses = plan(False, True)
            for slot in uses:
                dense(FINAL - 1, 0, NB - 1, uses, slot, NB - 1)


def experts(nc, io, dram):
    with ExitStack() as ctx:
        def sb(name, shape, dt=F32):
            return ctx.enter_context(nc.sbuf_tensor("x_" + name, shape, dt))

        def sem(name):
            return ctx.enter_context(nc.semaphore("x_" + name))

        ident = sb("ident", [P, P])
        w_gate, w_up = ([sb(f"{n}{p}", [P, DC, INNER]) for p in range(2)] for n in ("w_gate", "w_up"))
        w_down = [sb(f"w_down{p}", [P, MC, D]) for p in range(2)]
        rows = [sb(f"rows{p}", [SLOT_T, 2, XROW]) for p in range(2)]
        rows_t = [sb(f"rows_t{p}", [P, DC, CAP]) for p in range(2)]
        weight = [sb(f"weight{p}", [SLOT_T, 2]) for p in range(2)]
        index = [sb(f"index{p}", [SLOT_T, 2], I32) for p in range(2)]
        gate_e = [sb(f"gate_e{m}", [P, CAP]) for m in range(MC)]
        inner_t = [sb(f"inner_t{p}", [P, MC, CAP]) for p in range(2)]
        y = [sb(f"y{p}", [SLOT_T, 2, D]) for p in range(2)]
        ps_turn, ps_up, ps_y = ([ctx.enter_context(nc.psum_tensor(f"x_{n}{k}", [P, 512], F32)) for k in range(2)]
                                for n in ("ps_turn", "ps_up", "ps_y"))

        ident_in = sem("ident_in")
        rows_in, up_in, down_in = ([sem(f"{n}{p}") for p in range(2)] for n in ("rows_in", "up_in", "down_in"))
        turn_full, rows_t_done, up_full, gate_e_done = (
            sem(n) for n in ("turn_full", "rows_t_done", "up_full", "gate_e_done"))
        gate_step, inner_done, marks_done, down_full, y_done, added = (
            sem(n) for n in ("gate_step", "inner_done", "marks_done", "down_full", "y_done", "added"))
        passed = sem("passed")

        def for_experts(eng, one):
            for p in range(2):
                one(0, p)
            with eng.Fori(1, E // 2 - 1) as pair:
                for p in range(2):
                    one(pair, p)
            for p in range(2):
                one(E // 2 - 1, p, last=(p == 1))

        block = ctx.enter_context(nc.Block())

        @block.sync
        def _(sp):
            sp.dma_start(ident[:], io["c_ident"]).then_inc(ident_in, 16)

            def load(pair, p, last=False):
                e = pair * 2 + p
                if not (isinstance(pair, int) and pair == 0):
                    sp.wait_ge(turn_full, 2 * (e - 1))
                    sp.wait_ge(marks_done, e - 1)
                sp.dma_start(rows[p][:], dram["slots"][e].rearrange("(j p) x -> p j x", p=SLOT_T)).then_inc(rows_in[p], 16)
                if not (isinstance(pair, int) and pair == 0):
                    sp.wait_ge(up_full, MC * (e - 1))
                sp.dma_start(w_gate[p][:], io["w_gate"][e]).then_inc(up_in[p], 16)
                sp.dma_start(w_up[p][:], io["w_up"][e]).then_inc(up_in[p], 16)
                if not (isinstance(pair, int) and pair == 0):
                    sp.wait_ge(down_full, 2 * (e - 1))
                sp.dma_start(w_down[p][:], io["w_down"][e]).then_inc(down_in[p], 16)

            for_experts(sp, load)

        @block.tensor
        def _(pe):
            def turn(e, pair, p):
                pe.wait_ge(rows_in[p], 16 * (pair + 1))
                for j in range(2):
                    wait_from_1(pe, rows_t_done, 2 * (e - 1) + j + 1)
                    for c in range(DC):
                        mm = nc.tensor.transpose(ps_turn[j][:, c * SLOT_T:(c + 1) * SLOT_T],
                                                 rows[p][:, j, c * P:(c + 1) * P], ident[0:SLOT_T, 0:SLOT_T])
                    mm.then_inc(turn_full, 1)

            def expert(pair, p, last=False):
                e = pair * 2 + p
                pe.wait_ge(rows_t_done, 2 * (e + 1))
                pe.wait_ge(up_in[p], 32 * (pair + 1))
                for m in range(MC):
                    wait_from_1(pe, inner_done, MC * (e - 1) + m + 1)
                    for k, w in enumerate((w_gate[p], w_up[p])):
                        for c in range(DC):
                            mm = nc.tensor.matmul(ps_up[m][:, k * CAP:(k + 1) * CAP], w[:, c, m * P:(m + 1) * P],
                                                  rows_t[p][:, c, :], start=(c == 0), stop=(c == DC - 1))
                    mm.then_inc(up_full, 1)
                if not (isinstance(pair, int) and pair == 0 and p == 0):
                    down(e - 1, pair + p - 1, 1 - p)
                if not last:
                    turn(e + 1, pair + p, 1 - p)

            def down(e, pair, p):
                pe.wait_ge(down_in[p], 16 * (pair + 1))
                pe.wait_ge(inner_done, MC * (e + 1))
                for j in range(2):
                    wait_from_1(pe, y_done, 2 * (e - 1) + j + 1)
                    for m in range(MC):
                        mm = nc.tensor.matmul(ps_y[j][0:SLOT_T, :], inner_t[p][:, m, j * SLOT_T:(j + 1) * SLOT_T],
                                              w_down[p][:, m, :], start=(m == 0), stop=(m == MC - 1))
                    mm.then_inc(down_full, 1)

            pe.wait_ge(ident_in, 16)
            turn(0, 0, 0)
            for_experts(pe, expert)
            down(E - 1, E // 2 - 1, 1)

        @block.scalar
        def _(act):
            act.preload_act_table_set(EXP_LN_TABLES)

            def take_turned(e, p):
                for j in range(2):
                    act.wait_ge(turn_full, 2 * e + j + 1)
                    nc.scalar.activation(rows_t[p][:, :, j * SLOT_T:(j + 1) * SLOT_T],
                                         ps_turn[j][:, 0:DC * SLOT_T].rearrange("p (c m) -> p c m", c=DC),
                                         ACT.Identity).then_inc(rows_t_done, 1)

            def expert(pair, p, last=False):
                e = pair * 2 + p
                for m in range(MC):
                    act.wait_ge(up_full, MC * e + m + 1)
                    nc.scalar.activation(gate_e[m][:], ps_up[m][:, 0:CAP], ACT.Exp, scale=-1.0).then_inc(gate_e_done, 1)
                if not last:
                    take_turned(e + 1, 1 - p)

            take_turned(0, 0)
            for_experts(act, expert)

        @block.vector
        def _(dve):
            def take_marks(e, pair, p):
                dve.wait_ge(rows_in[p], 16 * (pair + 1))
                wait_from_1(dve, added, 32 * (e - 1))
                nc.vector.tensor_copy(weight[p][:].unsqueeze(2), rows[p][:, :, bass.ds(D + 1 + e, 1)])
                nc.vector.tensor_copy(index[p][:], rows[p][:, :, D]).then_inc(marks_done, 1)

            def expert(pair, p, last=False):
                e = pair * 2 + p
                chain = Chain(dve, gate_step, 3 * MC * e)
                for m in range(MC):
                    g, u = ps_up[m][:, 0:CAP], ps_up[m][:, CAP:2 * CAP]
                    dve.wait_ge(gate_e_done, MC * e + m + 1)
                    chain.done(nc.vector.tensor_scalar(gate_e[m][:], gate_e[m][:], 1.0, None, ALU.add))
                    chain.wait()
                    chain.done(nc.vector.reciprocal(gate_e[m][:], gate_e[m][:]))
                    chain.wait()
                    chain.done(nc.vector.tensor_tensor(gate_e[m][:], g, gate_e[m][:], ALU.mult))
                    chain.wait()
                    nc.vector.tensor_tensor(inner_t[p][:, m, :], u, gate_e[m][:], ALU.mult).then_inc(inner_done, 1)
                if not (isinstance(pair, int) and pair == 0 and p == 0):
                    weigh(e - 1, 1 - p)
                if not last:
                    take_marks(e + 1, pair + p, 1 - p)

            def weigh(e, p):
                dve.wait_ge(marks_done, e + 1)
                if not (isinstance(e, int) and e < 2):
                    dve.wait_ge(added, 32 * (e - 1))
                for j in range(2):
                    dve.wait_ge(down_full, 2 * e + j + 1)
                    nc.vector.tensor_scalar(y[p][:, j, :], ps_y[j][0:SLOT_T, :], weight[p][:, j:j + 1], None,
                                            ALU.mult).then_inc(y_done, 1)

            take_marks(0, 0, 0)
            for_experts(dve, expert)
            weigh(E - 1, 1)

        @block.gpsimd
        def _(pool):
            def add(pair, p, last=False):
                e = pair * 2 + p
                for j in range(2):
                    wait_apart(pool, y_done, 2 * e + j + 1, passed)
                    wait_apart(pool, added, 16 * (2 * e + j), passed)
                    nc.gpsimd.indirect_dma_start(
                        io["out"], bass.IndirectOffsetOnAxis(ap=index[p][:, j:j + 1], axis=0), y[p][:, j, :],
                        None, compute_op=ALU.add).then_inc(added, 16)

            for_experts(pool, add)
            pool.wait_ge(added, 32 * E)


def build(nc, io):
    dram = {
        "hidden": nc.dram_tensor("d_hidden", (NB, T, D), F32, kind="Internal").ap(),
        "normed_t": nc.dram_tensor("d_normed_t", (NB, P, DC, T), F32, kind="Internal").ap(),
        "slots": nc.dram_tensor("d_slots", (E, CAP, XROW), F32, kind="Internal").ap(),
        "q_parts": nc.dram_tensor("d_q_parts", (2, HG, 3, HD, T), BF16, kind="Internal").ap(),
        "k_parts": nc.dram_tensor("d_k_parts", (2, HG, 4, HD, T), BF16, kind="Internal").ap(),
    }
    embed(nc, io, dram)
    attend(nc, io, dram)
    experts(nc, io, dram)


def layout(inputs):
    import numpy as np
    a = {k: np.asarray(v) for k, v in inputs.items()}

    def rows(v):
        return np.ascontiguousarray(np.broadcast_to(v, (P,) + v.shape))

    def chunked(w):
        return np.ascontiguousarray(w.T.reshape(w.shape[1] // P, P, w.shape[0]).transpose(1, 0, 2))

    def chunked3(w):
        n, o, i = w.shape
        return np.ascontiguousarray(w.transpose(0, 2, 1).reshape(n, i // P, P, o).transpose(0, 2, 1, 3))

    i = np.arange(P, dtype=np.float32)[:, None]
    j = np.arange(T, dtype=np.float32)[None, :]
    query = np.float32(NT * P - P) + i
    decay = np.where(j <= query, j - query, np.float32(NEG)).astype(np.float32)
    tile = np.float32(P) * (j // P)
    ones = np.ones((1, T), np.float32)
    arrays = {
        "xT": np.ascontiguousarray(a["x"].reshape(NB * NT, P).T),
        "table": np.concatenate([a["L0_tok_frequencies"], a["L0_tok_phases"], a["L0_tok_amplitudes"],
                                 a["L0_tok_token_bias"]], axis=1),
        "w_projT": np.ascontiguousarray(a["L0_tok_W_proj"].T),
        "b_proj": rows(a["L0_tok_b_proj"]), "o_b": rows(a["L0_attn_o_b"]), "v_b": rows(a["L0_attn_v_b"]),
        "q_b": np.ascontiguousarray(a["L0_attn_q_b"].reshape(G, P).T),
        "k_b": np.ascontiguousarray(a["L0_attn_k_b"].reshape(G, P).T),
        "router_b": rows(a["L0_ffn_bias"]),
        "q_w": chunked(a["L0_attn_q_w"]), "k_w": chunked(a["L0_attn_k_w"]), "v_w": chunked(a["L0_attn_v_w"]),
        "o_w": chunked(a["L0_attn_o_w"]), "router_w": chunked(a["L0_ffn_gate_w"]),
        "sg": chunked(a["L0_ffn_sg"]), "su": chunked(a["L0_ffn_su"]), "sd": chunked(a["L0_ffn_sd"]),
        "w_gate": chunked3(a["L0_ffn_w_gate"]), "w_up": chunked3(a["L0_ffn_w_up"]),
        "w_down": chunked3(a["L0_ffn_w_down"]),
        "c_ident": np.eye(P, dtype=np.float32),
        "c_before": np.triu(np.ones((P, P), np.float32), 1),
        "c_position": np.arange(T, dtype=np.float32).reshape(NT, P).T.copy(),
        "c_spare": TOKENS + np.arange(CAP, dtype=np.float32).reshape(2, SLOT_T).T.copy(),
        "c_token": np.arange(2 * P, dtype=np.float32).reshape(2, P).T.copy(),
        "c_experts": rows(np.arange(E, dtype=np.float32)),
        "c_decay": decay,
        "c_query_rows": np.concatenate([-ones, -ones, -ones, tile, j % P]),
        "c_key_rows": np.concatenate([0 * ones, j % P, tile, ones, ones]),
    }
    return arrays


def kernel(**inputs):
    import concourse.bacc as bacc
    from concourse.bass_utils import run_bass_kernel_spmd

    nc = bacc.Bacc("TRN2", target_bir_lowering=False, num_devices=1)
    arrays = layout(inputs)
    io = {name: nc.dram_tensor(name, v.shape, mybir.dt.from_np(v.dtype), kind="ExternalInput").ap()
          for name, v in arrays.items()}
    io["out"] = nc.dram_tensor("out", (TOKENS + CAP, D), F32, kind="ExternalOutput").ap()
    build(nc, io)
    result = run_bass_kernel_spmd(nc, [arrays], core_ids=[0])
    return result.results[0]["out"][:TOKENS].reshape(NB, T, D)
```
